# Optimizing a Trainium2 kernel written in Bass

```python
import numpy as np
import jax
import jax.numpy as jnp

def _softmax(x, axis=-1):
    return jax.nn.softmax(x, axis=axis)

def _gelu(x):
    return jax.nn.gelu(x, approximate=True)

def _silu(x):
    return jax.nn.silu(x)

def _sigmoid(x):
    return jax.nn.sigmoid(x)

def _layernorm(x, axis=-1, eps=1e-05):
    m = jnp.mean(x, axis=axis, keepdims=True)
    v = jnp.var(x, axis=axis, keepdims=True)
    return (x - m) / jnp.sqrt(v + eps)

def _scatter_add(tgt, idx, src, axis=0):
    return tgt.at[idx].add(src)

def _segment_sum(src, seg, n):
    return jax.ops.segment_sum(src, seg, n)
kernel_name = 'mk_cond_resid_d2_seqx_r4_7d242a'

def setup_inputs(seed: int=0):
    np.random.seed(seed)
    _w = jnp.asarray

    def _rec_inputs():
        import jax
        import jax.numpy as jnp
        _rk = jax.random.key(seed)
        x = -0.0003929 + 0.9999 * jax.random.normal(jax.random.fold_in(_rk, 1), (2, 1024, 256), jnp.float32)
        _lenS = 1024 - jax.random.randint(jax.random.fold_in(_rk, 7), (2,), 0, max(1, 1024 // 4) + 1, jnp.int32)
        _lenS2 = 1024 - jax.random.randint(jax.random.fold_in(_rk, 8), (2,), 0, max(1, 1024 // 4) + 1, jnp.int32)
        cond_256 = -0.0209273 + 1.04763 * jax.random.normal(jax.random.fold_in(_rk, 11), (2, 64), jnp.float32)
        return (x, cond_256)
    x, cond_256 = _rec_inputs()

    def _L0_cond_setup():
        import jax, jax.numpy as jnp
        import numpy as np
        EPS = 1e-08

        def hamilton(q1, q2):
            w1, x1, y1, z1 = (q1[..., i, :] for i in range(4))
            w2, x2, y2, z2 = (q2[..., i, :] for i in range(4))
            w = w1 * w2 - x1 * x2 - y1 * y2 - z1 * z2
            x = w1 * x2 + x1 * w2 + y1 * z2 - z1 * y2
            y = w1 * y2 - x1 * z2 + y1 * w2 + z1 * x2
            z = w1 * z2 + x1 * y2 - y1 * x2 + z1 * w2
            return jnp.stack([w, x, y, z], axis=-2)

        def _normalize(q):
            return q / jnp.sqrt(jnp.sum(q * q, axis=0, keepdims=True) + EPS)
        key = jax.random.key(seed)
        k1, k2, k3, k4 = jax.random.split(key, 4)
        B, T, d_model = (4, 1024, 256)
        quat_dim = d_model // 4
        x = jax.random.normal(k1, (B, T, d_model), dtype=jnp.float32)
        q_left = jax.random.normal(k2, (4, quat_dim), dtype=jnp.float32)
        q_right = jax.random.normal(k3, (4, quat_dim), dtype=jnp.float32)
        spectral_gate = jax.random.uniform(k4, (1, 1, 1, quat_dim), dtype=jnp.float32)
        return {'x': x, 'q_left': q_left, 'q_right': q_right, 'spectral_gate': spectral_gate}
    _L0_cond_all = _L0_cond_setup()
    _L0_cond_in = {k: v for k, v in _L0_cond_all.items() if k in ('q_right', 'spectral_gate')}
    del _L0_cond_all

    def _L1_cond_setup():
        import jax, jax.numpy as jnp
        import numpy as np
        TOP_K = 2
        EPS = 1e-06
        B, S, H, G, E, M = (2, 512, 256, 64, 8, 512)
        key = jax.random.key(seed)
        ks = jax.random.split(key, 16)
        s_h = 1.0 / np.sqrt(H)
        s_g = 1.0 / np.sqrt(G)
        s_m = 1.0 / np.sqrt(M)
        return {'x': jax.random.normal(ks[0], (B, S, H), jnp.float32), 'genre_embed': jax.random.normal(ks[1], (B, 1, G), jnp.float32), 'rms_w': jnp.ones((H,), jnp.float32), 'wg_W': jax.random.normal(ks[2], (H, E), jnp.float32) * s_h, 'wg_b': jnp.zeros((E,), jnp.float32), 'gg_W': jax.random.normal(ks[3], (G, E), jnp.float32) * s_g, 'gg_b': jnp.zeros((E,), jnp.float32), 'W1': jax.random.normal(ks[4], (E, H, M), jnp.float32) * s_h, 'b1': jnp.zeros((E, M), jnp.float32), 'W2': jax.random.normal(ks[5], (E, M, M), jnp.float32) * s_m, 'b2': jnp.zeros((E, M), jnp.float32), 'W3': jax.random.normal(ks[6], (E, M, H), jnp.float32) * s_m, 'b3': jnp.zeros((E, H), jnp.float32)}
    _L1_cond_all = _L1_cond_setup()
    _L1_cond_in = {k: v for k, v in _L1_cond_all.items() if k in ('rms_w', 'wg_W', 'wg_b', 'gg_W', 'gg_b', 'W1', 'b1', 'W2', 'b2', 'W3', 'b3')}
    del _L1_cond_all
    return {'x': x, 'cond_256': cond_256, 'L0_cond_q_right': _L0_cond_in['q_right'], 'L0_cond_spectral_gate': _L0_cond_in['spectral_gate'], 'L1_cond_rms_w': _L1_cond_in['rms_w'], 'L1_cond_wg_W': _L1_cond_in['wg_W'], 'L1_cond_wg_b': _L1_cond_in['wg_b'], 'L1_cond_gg_W': _L1_cond_in['gg_W'], 'L1_cond_gg_b': _L1_cond_in['gg_b'], 'L1_cond_W1': _L1_cond_in['W1'], 'L1_cond_b1': _L1_cond_in['b1'], 'L1_cond_W2': _L1_cond_in['W2'], 'L1_cond_b2': _L1_cond_in['b2'], 'L1_cond_W3': _L1_cond_in['W3'], 'L1_cond_b3': _L1_cond_in['b3']}

def reference(x, cond_256, L0_cond_q_right, L0_cond_spectral_gate, L1_cond_rms_w, L1_cond_wg_W, L1_cond_wg_b, L1_cond_gg_W, L1_cond_gg_b, L1_cond_W1, L1_cond_b1, L1_cond_W2, L1_cond_b2, L1_cond_W3, L1_cond_b3):
    import jax
    import jax.numpy as jnp

    def _L0_cond_ref(x, q_left, q_right, spectral_gate):
        import jax, jax.numpy as jnp
        import numpy as np
        EPS = 1e-08

        def hamilton(q1, q2):
            w1, x1, y1, z1 = (q1[..., i, :] for i in range(4))
            w2, x2, y2, z2 = (q2[..., i, :] for i in range(4))
            w = w1 * w2 - x1 * x2 - y1 * y2 - z1 * z2
            x = w1 * x2 + x1 * w2 + y1 * z2 - z1 * y2
            y = w1 * y2 - x1 * z2 + y1 * w2 + z1 * x2
            z = w1 * z2 + x1 * y2 - y1 * x2 + z1 * w2
            return jnp.stack([w, x, y, z], axis=-2)

        def _normalize(q):
            return q / jnp.sqrt(jnp.sum(q * q, axis=0, keepdims=True) + EPS)
        B, T, d_model = x.shape
        quat_dim = d_model // 4
        x_quat = x.reshape(B, T, 4, quat_dim)
        x_spectral = jnp.fft.fft(x_quat, axis=1)
        x_filtered = jnp.fft.ifft(x_spectral * spectral_gate, axis=1).real.astype(x.dtype)
        q_left_n = _normalize(q_left)
        q_right_n = _normalize(q_right)
        conj_sign = jnp.array([1.0, -1.0, -1.0, -1.0], dtype=x.dtype)[:, None]
        q_right_conj = q_right_n * conj_sign
        x_right = hamilton(x_filtered, q_right_conj)
        x_rotated = hamilton(q_left_n, x_right)
        return x_rotated.reshape(B, T, d_model)

    def _L1_cond_ref(x, genre_embed, rms_w, wg_W, wg_b, gg_W, gg_b, W1, b1, W2, b2, W3, b3):
        import jax, jax.numpy as jnp
        import numpy as np
        TOP_K = 2
        EPS = 1e-06
        E = W1.shape[0]
        var = jnp.mean(x * x, axis=-1, keepdims=True)
        xn = rms_w * (x * jax.lax.rsqrt(var + EPS))
        gate = xn @ wg_W + wg_b + (genre_embed @ gg_W + gg_b)
        gate_w = jax.nn.softmax(gate, axis=-1)
        topk_w, topk_i = jax.lax.top_k(gate_w, TOP_K)
        cw = jnp.sum(jax.nn.one_hot(topk_i, E, dtype=x.dtype) * topk_w[..., None], axis=-2)
        h1 = jax.nn.relu(jnp.einsum('bsh,ehm->bsem', x, W1) + b1)
        h2 = jax.nn.relu(jnp.einsum('bsem,emn->bsen', h1, W2) + b2)
        out_e = jnp.einsum('bsen,enh->bseh', h2, W3) + b3
        return jnp.einsum('bseh,bse->bsh', out_e, cw)
    x = x + _L0_cond_ref(x, cond_256, L0_cond_q_right, L0_cond_spectral_gate)
    x = x + _L1_cond_ref(x, cond_256[:, None, :], L1_cond_rms_w, L1_cond_wg_W, L1_cond_wg_b, L1_cond_gg_W, L1_cond_gg_b, L1_cond_W1, L1_cond_b1, L1_cond_W2, L1_cond_b2, L1_cond_W3, L1_cond_b3)
    return x

_drawn_inputs = setup_inputs


def setup_inputs(seed=0):
    import zlib

    import numpy as np

    out = dict(_drawn_inputs(seed))
    spreads = {'L1_cond_rms_w': (1.0, 0.2),
     'L1_cond_wg_b': (0.0, 0.1),
     'L1_cond_gg_b': (0.0, 0.1),
     'L1_cond_b1': (0.0, 0.412),
     'L1_cond_b2': (0.0, 0.287),
     'L1_cond_b3': (0.0, 0.1)}
    factors = {}
    for name, (base, spread) in spreads.items():
        noise = np.random.default_rng([zlib.crc32(name.encode()), seed]).standard_normal(out[name].shape)
        drawn = base * np.exp(spread * noise) if base else spread * noise
        out[name] = jnp.asarray(drawn.astype(out[name].dtype))
    for name, factor in factors.items():
        out[name] = (out[name] * factor).astype(out[name].dtype)
    return out
```

```python
import concourse.bass as bass
from concourse import mybir
from contextlib import ExitStack

BATCH, SEQ, H, GENRE, EXPERTS, M = 2, 1024, 256, 64, 8, 512
P = 128
TOKENS = BATCH * SEQ
TILES = TOKENS // P
QD = H // 4
TOP = 2
KH, KM = H // P, M // P
WIDE = 2 * P
MAX_TILES = TOKENS * TOP // WIDE + EXPERTS - 1
COLS = 2 * (MAX_TILES + 1)
PICKS = TOP * TILES
PAD_ROWS = 2 * P
ROWS = TOKENS + PAD_ROWS
XW = H + EXPERTS

O_W1, O_W2, O_W3 = 0, KH * M, KH * M + KM * M
O_B1 = O_W3 + KM * H
O_B2 = O_B1 + KM
PACK = O_B2 + KM

SMALL = dict(cond2=2, q=8, lx=16, gain=1, rms=4, wg=4 * EXPERTS)
CONST = dict(ident=P, before=P, ones=P, diag=QD, iota=P, token=TILES, pad=COLS,
             lsign=16, rsign=8, same=8, eps=2)


def columns(widths):
    at, out = 0, {}
    for name, n in widths.items():
        out[name] = (at, at + n)
        at += n
    return out, at


def build(nc, xT, small, cst_in_ap, ctx_in, wpack, b3, out):
    f32, bf16, i32, u32 = mybir.dt.float32, mybir.dt.bfloat16, mybir.dt.int32, mybir.dt.uint32
    ALU = mybir.AluOpType
    ACT = mybir.ActivationFunctionType
    AX = mybir.AxisListType.X
    S, NS = columns(SMALL)
    C, NC_ = columns(CONST)

    ctx = ExitStack()
    with ctx:
        def sb(name, shape, dt=f32):
            return ctx.enter_context(nc.sbuf_tensor(name, shape, dt))

        def sem(name):
            return ctx.enter_context(nc.semaphore(name))

        x1_rows = nc.dram_tensor("x1_rows", [ROWS, H], f32).ap()

        xT_sb = sb("xT_sb", [P, KH, TOKENS])
        small_sb = sb("small_sb", [P, NS])
        cst_sb = sb("cst_sb", [P, NC_])
        ctx_sb = sb("ctx_sb", [GENRE + 2, BATCH * P + EXPERTS])
        weights = sb("weights", [P, 2, PACK])
        b3_sb = sb("b3_sb", [P, 2, H])

        squares = sb("squares", [P, 6])
        norms = sb("norms", [P, 2])
        roots = sb("roots", [P, 2])
        inverse = sb("inverse", [P, 2])
        gain = sb("gain", [P, 2])
        left = sb("left", [P, 16])
        right = sb("right", [P, 8])
        products = sb("products", [P, 2, 4, 4])
        coef = sb("coef", [P, 2, 4])
        gw_rms = sb("gw_rms", [P, 4, EXPERTS])
        gw_prod = sb("gw_prod", [P, 2, EXPERTS, 4])
        mix = sb("mix", [P, KH, XW])

        x1 = sb("x1", [P, TILES, XW])
        sq_junk = sb("sq_junk", [P, 2, H])
        ssum = sb("ssum", [P, TILES])
        rms = sb("rms", [P, TILES])
        rstd = sb("rstd", [P, TILES])
        logit = sb("logit", [P, TILES, EXPERTS])
        shifted = sb("shifted", [P, TILES, EXPERTS])
        top_logit = sb("top_logit", [P, TILES])
        expo = sb("expo", [P, TILES, EXPERTS])
        esum = sb("esum", [P, TILES])
        einv = sb("einv", [P, TILES])
        gatew = sb("gatew", [P, TILES, EXPERTS])
        topw = sb("topw", [P, TILES, 8])
        topi = sb("topi", [P, TILES, 8], u32)
        chosen = sb("chosen", [P, TOP, TILES, EXPERTS])
        mask = sb("mask", [P, TILES, EXPERTS], bf16)
        before_bf = sb("before_bf", [P, P], bf16)
        ones_bf = sb("ones_bf", [P, P], bf16)
        cnt_up = sb("cnt_up", [P, EXPERTS], i32)
        cnt_sh = sb("cnt_sh", [P, EXPERTS], i32)
        ntile = sb("ntile", [P, EXPERTS])
        upto = sb("upto", [P, EXPERTS])
        base = sb("base", [P, EXPERTS])
        table = sb("table", [P, EXPERTS + 1], i32)
        pos = sb("pos", [P, TILES, EXPERTS])
        posm = sb("posm", [P, TOP, TILES, EXPERTS])
        slot_f = sb("slot_f", [P, PICKS])
        slot = sb("slot", [P, PICKS], i32)
        slot_col = sb("slot_col", [P, PICKS], i32)
        slot_row = sb("slot_row", [P, PICKS], i32)
        is_row = sb("is_row", [P, PICKS, P])
        is_col = sb("is_col", [P, PICKS, COLS])
        carried = sb("carried", [P, PICKS, 2 * COLS])
        slot_w = sb("slot_w", [P, COLS])
        slot_tok = sb("slot_tok", [P, COLS])
        pad_row = sb("pad_row", [P, COLS])
        slot_idx = sb("slot_idx", [P, COLS], i32)
        zeros = sb("zeros", [P, PAD_ROWS // P * H])

        gather_idx = sb("gather_idx", [P, 2], i32)
        scatter_idx = sb("scatter_idx", [P, 2], i32)
        xg = sb("xg", [P, 2, H])
        xs = sb("xs", [P, KH, WIDE])
        h1 = sb("h1", [P, KM, WIDE])
        h2 = sb("h2", [P, KM, WIDE])
        y = sb("y", [P, 2, H])
        yw = sb("yw", [P, 2, H])

        def bank(name):
            return ctx.enter_context(nc.psum_tensor(name, [P, 512], f32))

        ps_x = bank("ps_x")
        ps_h1 = [bank("ps_h1a"), bank("ps_h1b")]
        ps_h2 = [bank(f"ps_h2{m}") for m in range(KM)]
        ps_y = bank("ps_y")
        ps_x1 = ps_h1
        ps_rank, ps_ctx, ps_slots = ps_h2[0], ps_h2[1], ps_h2[2]

        def small_c(name):
            return small_sb[:, S[name][0]:S[name][1]]

        def cst(name):
            return cst_sb[:, C[name][0]:C[name][1]]

        small_in = sem("small_in")
        cst_in = sem("cst_in")
        ctx_in_sem = sem("ctx_loaded")
        XCH = 4
        x_in = [sem(f"x_in{n}") for n in range(XCH)]
        w_in = [sem("w_in_even"), sem("w_in_odd")]
        b3_in = [sem("b3_in_even"), sem("b3_in_odd")]
        rows_out = sem("rows_out")
        resid_out = sem("resid_out")
        dve_step = sem("dve_step")
        act_step = sem("act_step")
        norms_ready = sem("norms_ready")
        mix_ready = sem("mix_ready")
        bf_ready = sem("bf_ready")
        ctx_ready = sem("ctx_ready")
        x1_done = sem("x1_done")
        x1_copied = sem("x1_copied")
        ss_ready = sem("ss_ready")
        rms_ready = sem("rms_ready")
        shifted_ready = sem("shifted_ready")
        exp_ready = sem("exp_ready")
        mask_ready = sem("mask_ready")
        rank_done = sem("rank_done")
        table_ready = sem("table_ready")
        onehot_ready = sem("onehot_ready")
        slots_done = sem("slots_done")
        idx_ready = sem("idx_ready")
        zero_ready = sem("zero_ready")
        gidx_ready = sem("gidx_ready")
        gathered = sem("gathered")
        xpose_done = sem("xpose_done")
        xs_ready = sem("xs_ready")
        l1_done = sem("l1_done")
        h1_ready = sem("h1_ready")
        l2_done = sem("l2_done")
        h2_ready = sem("h2_ready")
        l3_done = sem("l3_done")
        y_biased = sem("y_biased")
        y_ready = sem("y_ready")
        sidx_ready = sem("sidx_ready")
        pool_fence = sem("pool_fence")
        scattered = sem("scattered")

        block = ctx.enter_context(nc.Block())

        def expert_tiles(eng, body, head=None):
            with eng.Fori(0, EXPERTS // 2) as pair:
                for par in range(2):
                    e = pair * 2 + par
                    eng.wait_ge(table_ready, 1)
                    if head is not None:
                        head(pair, par)
                    first = eng.value_load(table[0:1, bass.ds(e, 1)], min_val=0, max_val=MAX_TILES - 1)
                    end = eng.value_load(table[0:1, bass.ds(e + 1, 1)], min_val=1, max_val=MAX_TILES)
                    with eng.Fori(first, end) as g:
                        body(g, par)

        @block.sync
        def _(sp):
            sp.dma_start(small_sb[:, :], small).then_inc(small_in, 16)
            sp.dma_start(cst_sb[:, :], cst_in_ap).then_inc(cst_in, 16)
            sp.dma_start(ctx_sb[:, :], ctx_in).then_inc(ctx_in_sem, 16)
            n = TOKENS // XCH
            for c in range(XCH):
                sp.dma_start(xT_sb[:, :, c * n:(c + 1) * n],
                             xT[:, c * n:(c + 1) * n].rearrange("(k p) t -> p k t", p=P)).then_inc(x_in[c], 16)
            for par in range(2):
                sp.dma_start(weights[:, par, :], wpack[par, :, :]).then_inc(w_in[par], 16)
                sp.dma_start(b3_sb[:, par, :], b3[par:par + 1, :].to_broadcast([P, H])).then_inc(b3_in[par], 16)
            sp.wait_ge(zero_ready, 1)
            sp.dma_start(x1_rows[TOKENS:ROWS, :].rearrange("(p a) h -> p (a h)", p=P), zeros[:, :]).then_inc(rows_out, 16)
            sp.dma_start(out[TOKENS:ROWS, :].rearrange("(p a) h -> p (a h)", p=P), zeros[:, :]).then_inc(resid_out, 16)
            q = TILES // XCH
            for c in range(XCH):
                sp.wait_ge(x1_copied, (c + 1) * q)
                for dst, done in ((x1_rows, rows_out), (out, resid_out)):
                    sp.dma_start(dst[c * q * P:(c + 1) * q * P, :].rearrange("(t p) h -> p t h", p=P),
                                 x1[:, c * q:(c + 1) * q, 0:H]).then_inc(done, 16)
            sp.wait_ge(table_ready, 1)
            with sp.Fori(1, EXPERTS // 2) as pair:
                for par in range(2):
                    e = pair * 2 + par
                    through = sp.value_load(table[0:1, bass.ds(e - 1, 1)], min_val=1, max_val=MAX_TILES)
                    sp.wait_ge(y_biased, through + 1)
                    sp.dma_start(weights[:, par, :], wpack[bass.ds(e, 1), :, :].rearrange("o p w -> (o p) w"))\
                        .then_inc(w_in[par], 16)
                    sp.dma_start(b3_sb[:, par, :], b3[bass.ds(e, 1), :].to_broadcast([P, H]))\
                        .then_inc(b3_in[par], 16)

        @block.gpsimd
        def _(pool):
            pool.memset(zeros[:, :], 0.0).then_inc(zero_ready, 1)
            pool.wait_ge(idx_ready, 1)

            def gather(g):
                nc.gpsimd.tensor_copy(gather_idx[:, :], slot_idx[:, bass.ds(g * 2, 2)]).then_inc(gidx_ready, 1)
                pool.wait_ge(rows_out, 16 * (XCH + 1))
                pool.wait_ge(gidx_ready, g + 1)
                pool.sem_inc(pool_fence, 1)
                for k in range(2):
                    nc.gpsimd.indirect_dma_start(
                        out=xg[:, k, :], out_offset=None, in_=x1_rows,
                        in_offset=bass.IndirectOffsetOnAxis(ap=gather_idx[:, k:k + 1].bitcast(u32), axis=0))\
                        .then_inc(gathered, 16)

            gather(0)

            pool.wait_ge(resid_out, 16 * (XCH + 1))
            for k in range(2):
                nc.gpsimd.indirect_dma_start(
                    out=out, out_offset=bass.IndirectOffsetOnAxis(
                        ap=slot_idx[:, COLS - 2 + k:COLS - 1 + k].bitcast(u32), axis=0),
                    in_=zeros[:, 0:H], in_offset=None, compute_op=ALU.add).then_inc(scattered, 16)

            def body(g, par):
                pool.wait_ge(xpose_done, g + 1)
                pool.wait_ge(gathered, g * 32 + 32)
                gather(g + 1)
                pool.wait_ge(scattered, g * 32 + 32)
                nc.gpsimd.tensor_copy(scatter_idx[:, :], slot_idx[:, bass.ds(g * 2, 2)]).then_inc(sidx_ready, 1)
                pool.wait_ge(sidx_ready, g + 1)
                pool.wait_ge(resid_out, 16 * (XCH + 1))
                pool.wait_ge(y_ready, g * 2 + 2)
                pool.sem_inc(pool_fence, 1)
                for k in range(2):
                    nc.gpsimd.indirect_dma_start(
                        out=out, out_offset=bass.IndirectOffsetOnAxis(ap=scatter_idx[:, k:k + 1].bitcast(u32), axis=0),
                        in_=yw[:, k, :], in_offset=None, compute_op=ALU.add).then_inc(scattered, 16)

            expert_tiles(pool, body)
            tiles = pool.value_load(table[0:1, EXPERTS:EXPERTS + 1], min_val=1, max_val=MAX_TILES)
            pool.wait_ge(scattered, tiles * 32 + 32)
            pool.wait_ge(gathered, tiles * 32 + 32)

        @block.scalar
        def _(act):
            act.wait_ge(cst_in, 16)
            act.wait_ge(norms_ready, 1)
            nc.scalar.activation(roots[:, :], norms[:, :], ACT.Sqrt, bias=cst("eps")[:, 0:1]).then_inc(act_step, 1)
            for t in range(TILES):
                act.wait_ge(x1_copied, t + 1)
                if t >= 2:
                    act.wait_ge(ss_ready, t - 1)
                nc.scalar.activation(sq_junk[:, t % 2, :], x1[:, t, 0:H], ACT.Square,
                                     accum_out=ssum[:, t:t + 1]).then_inc(ss_ready, 1)
            act.wait_ge(ss_ready, TILES)
            nc.scalar.activation(rms[:, :], ssum[:, :], ACT.Sqrt, bias=cst("eps")[:, 1:2],
                                 scale=1.0 / H).then_inc(rms_ready, 1)
            act.wait_ge(shifted_ready, 1)
            nc.scalar.activation(expo[:, :, :], shifted[:, :, :], ACT.Exp).then_inc(exp_ready, 1)
            def head(pair, par):
                act.wait_ge(w_in[par], pair * 16 + 16)

            def body(g, par):
                for src, dst, done, ready, off in ((ps_h1, h1, l1_done, h1_ready, O_B1),
                                                   (ps_h2, h2, l2_done, h2_ready, O_B2)):
                    for m in range(KM):
                        act.wait_ge(done, g * KM + (m + 1))
                        nc.scalar.activation(dst[:, m, :], src[m % len(src)][:, 0:WIDE], ACT.Relu,
                                             bias=weights[:, par, off + m:off + m + 1]).then_inc(ready, 1)

            expert_tiles(act, body, head)

        @block.vector
        def _(dve):
            steps = [0]

            def link(ins):
                steps[0] += 1
                ins.then_inc(dve_step, 1)
                dve.wait_ge(dve_step, steps[0])

            V = nc.vector
            dve.wait_ge(small_in, 16)
            link(V.tensor_tensor(squares[:, :], small_sb[:, 0:6], small_sb[:, 0:6], ALU.mult))
            V.tensor_reduce(norms[:, 0:1], squares[:, 0:2], AX, ALU.add)
            V.tensor_reduce(norms[:, 1:2], squares[:, 2:6], AX, ALU.add).then_inc(norms_ready, 1)
            dve.wait_ge(cst_in, 16)
            link(V.tensor_tensor(left[:, :], small_c("lx"), cst("lsign"), ALU.mult))
            link(V.tensor_tensor(right[:, :], small_c("q"), cst("rsign"), ALU.mult))
            link(V.tensor_tensor(
                products[:, :, :, :],
                left[:, :].rearrange("p (a i k) -> p a i k", a=1, i=4).to_broadcast([P, 2, 4, 4]),
                right[:, :].rearrange("p (b a k) -> p b a k", b=2, a=1).to_broadcast([P, 2, 4, 4]), ALU.mult))
            link(V.tensor_reduce(coef[:, :, :], products[:, :, :, :], AX, ALU.add))
            dve.wait_ge(act_step, 1)
            link(V.reciprocal(inverse[:, :], roots[:, :]))
            link(V.tensor_tensor(gain[:, 0:1], inverse[:, 0:1], inverse[:, 1:2], ALU.mult))
            link(V.tensor_tensor(gain[:, 1:2], gain[:, 0:1], small_c("gain"), ALU.mult))
            link(V.scalar_tensor_tensor(coef[:, :, :], coef[:, :, :], gain[:, 1:2],
                                        cst("same").rearrange("p (b i) -> p b i", b=2), ALU.mult, ALU.add))
            link(V.tensor_tensor(
                mix[:, :, 0:H].rearrange("p b (i d) -> p b i d", i=4),
                cst("diag").rearrange("p (a c d) -> p a c d", a=1, c=1).to_broadcast([P, 2, 4, QD]),
                coef[:, :, :].rearrange("p b (i a) -> p b i a", a=1).to_broadcast([P, 2, 4, QD]), ALU.mult))
            link(V.tensor_tensor(gw_rms[:, :, :], small_c("wg").rearrange("p (i e) -> p i e", i=4),
                                 small_c("rms").rearrange("p (i a) -> p i a", a=1).to_broadcast([P, 4, EXPERTS]),
                                 ALU.mult))
            link(V.tensor_tensor(
                gw_prod[:, :, :, :],
                gw_rms[:, :, :].rearrange("p i (a e) -> p a e i", a=1).to_broadcast([P, 2, EXPERTS, 4]),
                coef[:, :, :].rearrange("p b (a i) -> p b a i", a=1).to_broadcast([P, 2, EXPERTS, 4]), ALU.mult))
            V.tensor_reduce(mix[:, :, H:XW], gw_prod[:, :, :, :], AX, ALU.add).then_inc(mix_ready, 1)
            V.tensor_copy(before_bf[:, :], cst("before")).then_inc(bf_ready, 1)
            V.tensor_copy(ones_bf[:, :], cst("ones")).then_inc(bf_ready, 1)

            for t in range(TILES):
                dve.wait_ge(x1_done, t + 1)
                V.tensor_copy(x1[:, t, :], ps_x1[t % 2][:, 0:XW]).then_inc(x1_copied, 1)

            dve.wait_ge(x1_copied, TILES)
            dve.wait_ge(rms_ready, 1)
            link(V.reciprocal(rstd[:, :], rms[:, :]))

            def over_experts(ap):
                return ap.rearrange("p (t a) -> p t a", a=1).to_broadcast([P, TILES, EXPERTS])

            link(V.tensor_tensor(logit[:, :, :], x1[:, :, H:XW], over_experts(rstd[:, :]), ALU.mult))
            dve.wait_ge(ctx_ready, 1)
            lg = logit[:, :, :].rearrange("p (b t) e -> p b t e", b=BATCH)
            link(V.tensor_tensor(
                lg, lg, ps_ctx[:, 0:BATCH * EXPERTS].rearrange("p (b a e) -> p b a e", b=BATCH, a=1)
                .to_broadcast([P, BATCH, TILES // BATCH, EXPERTS]), ALU.add))
            link(V.tensor_reduce(top_logit[:, :], logit[:, :, :], AX, ALU.max))
            V.tensor_tensor(shifted[:, :, :], logit[:, :, :], over_experts(top_logit[:, :]), ALU.subtract)\
                .then_inc(shifted_ready, 1)
            dve.wait_ge(exp_ready, 1)
            link(V.tensor_reduce(esum[:, :], expo[:, :, :], AX, ALU.add))
            link(V.reciprocal(einv[:, :], esum[:, :]))
            link(V.tensor_tensor(gatew[:, :, :], expo[:, :, :], over_experts(einv[:, :]), ALU.mult))
            for t in range(TILES):
                last = V.max(topw[:, t, :], gatew[:, t, :])
            link(last)
            for t in range(TILES):
                last = V.max_index(topi[:, t, :], topw[:, t, :], gatew[:, t, :])
            link(last)
            iota = cst("iota")
            link(V.tensor_tensor(
                chosen[:, :, :, :],
                iota[:, 0:EXPERTS].rearrange("p (a b e) -> p a b e", a=1, b=1).to_broadcast([P, TOP, TILES, EXPERTS]),
                topi[:, :, 0:TOP].rearrange("p t (k a) -> p k t a", a=1).to_broadcast([P, TOP, TILES, EXPERTS]),
                ALU.is_equal))
            V.tensor_tensor(mask[:, :, :], chosen[:, 0, :, :], chosen[:, 1, :, :], ALU.add).then_inc(mask_ready, 1)
            dve.wait_ge(rank_done, 1)
            link(V.tensor_scalar(cnt_up[:, :], ps_rank[:, TILES * EXPERTS:(TILES + 1) * EXPERTS],
                                 float(WIDE - 1), None, ALU.add))
            link(V.tensor_scalar(cnt_sh[:, :], cnt_up[:, :], 8, None, ALU.logical_shift_right))
            link(V.tensor_scalar(ntile[:, :], cnt_sh[:, :], 1.0, None, ALU.max))
            link(V.tensor_tensor_scan(upto[:, :], cst("ones")[:, 0:EXPERTS], ntile[:, :], 0.0, ALU.mult, ALU.add))
            link(V.tensor_tensor(base[:, :], upto[:, :], ntile[:, :], ALU.subtract))
            V.tensor_copy(table[:, 0:EXPERTS], base[:, :])
            V.tensor_copy(table[:, EXPERTS:EXPERTS + 1], upto[:, EXPERTS - 1:EXPERTS]).then_inc(table_ready, 1)
            link(V.scalar_tensor_tensor(
                pos[:, :, :], base[:, :].rearrange("p (a e) -> p a e", a=1).to_broadcast([P, TILES, EXPERTS]),
                float(WIDE), ps_rank[:, 0:TILES * EXPERTS].rearrange("p (t e) -> p t e", e=EXPERTS),
                ALU.mult, ALU.add))
            link(V.tensor_tensor(
                posm[:, :, :, :], chosen[:, :, :, :],
                pos[:, :, :].rearrange("p (a t) e -> p a t e", a=1).to_broadcast([P, TOP, TILES, EXPERTS]), ALU.mult))
            link(V.tensor_reduce(slot_f[:, :].rearrange("p (k t) -> p k t", k=TOP), posm[:, :, :, :], AX, ALU.add))
            link(V.tensor_copy(slot[:, :], slot_f[:, :]))
            link(V.tensor_scalar(slot_col[:, :], slot[:, :], 7, None, ALU.logical_shift_right))
            link(V.tensor_scalar(slot_row[:, :], slot[:, :], P - 1, None, ALU.bitwise_and))
            link(V.tensor_tensor(
                is_col[:, :, :], iota[:, 0:COLS].rearrange("p (a c) -> p a c", a=1).to_broadcast([P, PICKS, COLS]),
                slot_col[:, :].rearrange("p (n a) -> p n a", a=1).to_broadcast([P, PICKS, COLS]), ALU.is_equal))
            for k in range(TOP):
                n0, n1 = k * TILES, (k + 1) * TILES
                V.tensor_tensor(carried[:, n0:n1, 0:COLS], is_col[:, n0:n1, :],
                                cst("token").rearrange("p (t a) -> p t a", a=1).to_broadcast([P, TILES, COLS]),
                                ALU.mult)
                V.tensor_tensor(carried[:, n0:n1, COLS:2 * COLS], is_col[:, n0:n1, :],
                                topw[:, :, k:k + 1].to_broadcast([P, TILES, COLS]), ALU.mult)
            for n in range(PICKS):
                V.tensor_scalar(is_row[:, n, :], iota, slot_row[:, n:n + 1], None, ALU.is_equal)\
                    .then_inc(onehot_ready, 1)
            dve.wait_ge(slots_done, 1)
            link(V.scalar_tensor_tensor(pad_row[:, :], ps_slots[:, 0:COLS], 0.0, cst("pad"), ALU.is_equal, ALU.mult))
            V.tensor_copy(slot_w[:, :], ps_slots[:, COLS:2 * COLS])
            V.scalar_tensor_tensor(slot_idx[:, :], ps_slots[:, 0:COLS], -1.0, pad_row[:, :], ALU.add, ALU.add)\
                .then_inc(idx_ready, 1)

            def split_x():
                V.tensor_copy(xs[:, :, :], ps_x[:, :].rearrange("p (k s) -> p k s", k=KH)).then_inc(xs_ready, 1)

            dve.sem_inc(y_biased, 1)
            dve.wait_ge(xpose_done, 1)
            split_x()

            def head(pair, par):
                dve.wait_ge(b3_in[par], pair * 16 + 16)

            def body(g, par):
                dve.wait_ge(xpose_done, g + 2)
                split_x()
                dve.wait_ge(l3_done, g + 1)
                V.tensor_tensor(y[:, :, :], ps_y[:, :].rearrange("p (k h) -> p k h", k=2),
                                b3_sb[:, par:par + 1, :].to_broadcast([P, 2, H]), ALU.add).then_inc(y_biased, 1)
                dve.wait_ge(y_biased, g + 2)
                dve.wait_ge(scattered, g * 32 + 32)
                for k in range(2):
                    V.tensor_scalar(yw[:, k, :], y[:, k, :], slot_w[:, bass.ds(g * 2 + k, 1)], None, ALU.mult)\
                        .then_inc(y_ready, 1)

            expert_tiles(dve, body, head)

        @block.tensor
        def _(pe):
            ident = cst("ident")
            pe.wait_ge(cst_in, 16)
            pe.wait_ge(ctx_in_sem, 16)
            for b in range(BATCH):
                last = nc.tensor.matmul(ps_ctx[:, b * EXPERTS:(b + 1) * EXPERTS], ctx_sb[:, b * P:(b + 1) * P],
                                        ctx_sb[:, BATCH * P:BATCH * P + EXPERTS], start=True, stop=True)
            last.then_inc(ctx_ready, 1)
            pe.wait_ge(mix_ready, 1)
            for t in range(TILES):
                if t % (TILES // XCH) == 0:
                    pe.wait_ge(x_in[t // (TILES // XCH)], 16)
                if t >= 2:
                    pe.wait_ge(x1_copied, t - 1)
                for k in range(KH):
                    last = nc.tensor.matmul(ps_x1[t % 2][:, 0:XW], xT_sb[:, k, t * P:(t + 1) * P], mix[:, k, :],
                                            start=(k == 0), stop=(k == KH - 1))
                last.then_inc(x1_done, 1)
            pe.wait_ge(mask_ready, 1)
            pe.wait_ge(bf_ready, 2)
            nc.tensor.matmul(ps_rank[:, 0:TILES * EXPERTS], before_bf[:, :], mask[:, :, :], start=True, stop=False,
                             skip_group_check=True)
            for t in range(TILES):
                last = nc.tensor.matmul(
                    ps_rank[:, (t + 1) * EXPERTS:(TILES + 1) * EXPERTS].rearrange("p (t e) -> p t e", e=EXPERTS),
                    ones_bf[:, :], mask[:, t:t + 1, :].to_broadcast([P, TILES - t, EXPERTS]),
                    start=False, stop=(t == TILES - 1), skip_group_check=True)
            last.then_inc(rank_done, 1)
            for n in range(PICKS):
                pe.wait_ge(onehot_ready, n + 1)
                last = nc.tensor.matmul(ps_slots[:, 0:2 * COLS], is_row[:, n, :], carried[:, n, :],
                                        start=(n == 0), stop=(n == PICKS - 1))
            last.then_inc(slots_done, 1)

            def transpose_x():
                for kb in range(KH):
                    for k in range(2):
                        last = nc.tensor.transpose(ps_x[:, kb * WIDE + k * P:kb * WIDE + (k + 1) * P],
                                                   xg[:, k, kb * P:(kb + 1) * P], ident)
                last.then_inc(xpose_done, 1)

            pe.wait_ge(gathered, 32)
            transpose_x()

            def head(pair, par):
                pe.wait_ge(w_in[par], pair * 16 + 16)

            def body(g, par):
                w = weights[:, par, :]
                pe.wait_ge(xs_ready, g + 1)
                for m in range(KM):
                    if m >= 2:
                        pe.wait_ge(h1_ready, g * KM + (m - 1))
                    for k in range(KH):
                        o = O_W1 + k * M + m * P
                        last = nc.tensor.matmul(ps_h1[m % 2][:, 0:WIDE], w[:, o:o + P], xs[:, k, :],
                                                start=(k == 0), stop=(k == KH - 1))
                    last.then_inc(l1_done, 1)
                half = KM // 2
                for ks, ms in [((k,), range(KM)) for k in range(half)] + [(range(half, KM), (m,)) for m in range(KM)]:
                    for m in ms:
                        for k in ks:
                            if m == 0:
                                pe.wait_ge(h1_ready, g * KM + (k + 1))
                            o = O_W2 + k * M + m * P
                            last = nc.tensor.matmul(ps_h2[m][:, 0:WIDE], w[:, o:o + P], h1[:, k, :],
                                                    start=(k == 0), stop=(k == KM - 1))
                        if ks[-1] == KM - 1:
                            last.then_inc(l2_done, 1)
                pe.wait_ge(gathered, g * 32 + 64)
                transpose_x()
                pe.wait_ge(y_biased, g + 1)
                for k in range(KM):
                    pe.wait_ge(h2_ready, g * KM + (k + 1))
                    for s in range(2):
                        o = O_W3 + k * H
                        last = nc.tensor.matmul(ps_y[:, s * H:(s + 1) * H], h2[:, k, s * P:(s + 1) * P], w[:, o:o + H],
                                                start=(k == 0 and s == 0), stop=(k == KM - 1), skip_group_check=True)
                last.then_inc(l3_done, 1)

            expert_tiles(pe, body, head)



def constants():
    import numpy as np
    S, n = columns(CONST)
    c = np.zeros((P, n), np.float32)

    def put(name, v):
        c[:, S[name][0]:S[name][1]] = v

    p = np.arange(P)
    put("ident", np.eye(P))
    put("before", p[:, None] < p[None, :])
    put("ones", 1.0)
    put("diag", (p[:, None] % QD) == np.arange(QD)[None, :])
    put("iota", p[None, :])
    put("token", np.arange(TILES)[None, :] * P + p[:, None] + 1)
    put("pad", TOKENS + 1 + p[:, None] + P * (np.arange(COLS)[None, :] % 2))
    ls = np.array([[1, -1, -1, -1], [1, 1, -1, 1], [1, 1, 1, -1], [1, -1, 1, 1]])
    rs = np.array([[1, -1, -1, -1], [1, 1, 1, -1], [1, -1, 1, 1], [1, 1, -1, 1]])
    conj = np.array([1, -1, -1, -1])
    put("lsign", ls.reshape(1, 16))
    j = 2 * np.arange(2)[None, :, None] + (p // QD)[:, None, None]
    k = np.arange(4)[None, None, :]
    put("rsign", (rs[k, j] * conj[k ^ j]).reshape(P, 8))
    put("same", (k == j).reshape(P, 8))
    put("eps", np.array([1e-8, 1e-6]))
    return c


def kernel(**inputs):
    import numpy as np
    import concourse.bacc as bacc
    from concourse.bass_utils import run_bass_kernel_spmd

    a = {k: np.asarray(v) for k, v in inputs.items()}
    x, cond = a["x"], a["cond_256"]
    d = np.arange(P) % QD
    half = np.arange(P) // QD
    row = np.minimum(np.arange(4), BATCH - 1)
    i, k = np.arange(4)[:, None], np.arange(4)[None, :]
    j = 2 * np.arange(2)[None, :, None] + half[:, None, None]
    q = a["L0_cond_q_right"][np.arange(4)[None, None, :] ^ j, d[:, None, None]].reshape(P, 8)
    lx = cond[row[i ^ k][None], d[:, None, None]].reshape(P, 16)
    rms = a["L1_cond_rms_w"].reshape(4, QD)[:, d].T
    wg = a["L1_cond_wg_W"].reshape(4, QD, EXPERTS)[:, d].transpose(1, 0, 2).reshape(P, 4 * EXPERTS)
    small = np.concatenate([cond[:, d].T, q, lx, a["L0_cond_spectral_gate"].reshape(QD)[d][:, None], rms, wg], 1)
    ctx = np.ones((GENRE + 2, BATCH * P + EXPERTS), np.float32)
    for b in range(BATCH):
        ctx[:GENRE, b * P:(b + 1) * P] = cond[b][:, None]
    ctx[:GENRE, BATCH * P:] = a["L1_cond_gg_W"]
    ctx[GENRE, BATCH * P:] = a["L1_cond_wg_b"]
    ctx[GENRE + 1, BATCH * P:] = a["L1_cond_gg_b"]

    def blocks(w):
        e, kk, n = w.shape
        return w.reshape(e, kk // P, P, n).transpose(0, 2, 1, 3).reshape(e, P, -1)

    def column(b):
        return b.reshape(EXPERTS, KM, P).transpose(0, 2, 1)

    wpack = np.concatenate([blocks(a["L1_cond_W1"]), blocks(a["L1_cond_W2"]), blocks(a["L1_cond_W3"]),
                            column(a["L1_cond_b1"]), column(a["L1_cond_b2"])], 2)
    arrays = {"xT": x.reshape(TOKENS, H).T, "small": small, "cst": constants(), "ctx": ctx, "wpack": wpack,
              "b3": a["L1_cond_b3"]}
    arrays = {f"in_{n}": np.ascontiguousarray(v) for n, v in arrays.items()}

    nc = bacc.Bacc("TRN2", target_bir_lowering=False, num_devices=1)
    args = [nc.dram_tensor(n, v.shape, mybir.dt.from_np(v.dtype), kind="ExternalInput").ap()
            for n, v in arrays.items()]
    out = nc.dram_tensor("out_rows", (ROWS, H), mybir.dt.float32, kind="ExternalOutput").ap()
    build(nc, *args, out)
    r = run_bass_kernel_spmd(nc, [arrays], core_ids=[0])
    return r.results[0]["out_rows"][:TOKENS].reshape(BATCH, SEQ, H)
```

```python
import concourse.bass as bass
from concourse import mybir
from collections import namedtuple
from contextlib import ExitStack

BATCH, SEQ, H, GENRE, EXPERTS, M = 2, 1024, 256, 64, 8, 512
P = 128
TOKENS = BATCH * SEQ
TILES = TOKENS // P
QD = H // 4
TOP = 2
KH, KM = H // P, M // P
WIDE = 2 * P
MAX_TILES = TOKENS * TOP // WIDE + EXPERTS - 1
COLS = 2 * (MAX_TILES + 3)
PICKS = TOP * TILES
PAD_SETS = 2
ROWS = TOKENS + PAD_SETS * P
XW = H + EXPERTS

O_W1, O_W2, O_W3 = 0, KH * M, KH * M + KM * M
PACK = O_W3 + KM * H
STEPS = ((0, 2816), (2816, PACK))
FIRST_STEPS = 8

SMALL = dict(cond2=2, q=8, lx=16, gain=1, rms=4, wg=4 * EXPERTS)
CONST = dict(ident=P, before=P, ones=P, diag=QD, iota=P, token=TILES, pad=COLS,
             lsign=16, rsign=8, same=8, eps=2)


WIDE_END_BIT, NARROW_BIT = 8, 16
Tile = namedtuple("Tile", "g pair expert first")


def columns(widths):
    at, out = 0, {}
    for name, n in widths.items():
        out[name] = (at, at + n)
        at += n
    return out, at


def build(nc, xT, small, cst_in_ap, ctx_in, wpack, bpack, b3, out):
    f32r = mybir.dt.float32r
    f32, bf16, i32, u32 = mybir.dt.float32, mybir.dt.bfloat16, mybir.dt.int32, mybir.dt.uint32
    ALU = mybir.AluOpType
    ACT = mybir.ActivationFunctionType
    AX = mybir.AxisListType.X
    S, NS = columns(SMALL)
    C, NC_ = columns(CONST)

    ctx = ExitStack()
    with ctx:
        def sb(name, shape, dt=f32):
            return ctx.enter_context(nc.sbuf_tensor(name, shape, dt))

        def sem(name):
            return ctx.enter_context(nc.semaphore(name))

        x1_rows = nc.dram_tensor("x1_rows", [ROWS, H], f32).ap()

        xT_sb = sb("xT_sb", [P, KH, TOKENS])
        small_sb = sb("small_sb", [P, NS])
        cst_sb = sb("cst_sb", [P, NC_])
        ctx_sb = sb("ctx_sb", [GENRE + 2, BATCH * P + EXPERTS])
        w_raw = sb("w_raw", [P, 2, PACK])
        w_hi = sb("w_hi", [P, 2, PACK], f32r)
        w_lo = sb("w_lo", [P, 2, PACK], f32r)
        bias_sb = sb("bias_sb", [P, EXPERTS, 2 * KM])
        b3_sb = sb("b3_sb", [P, EXPERTS, H])

        squares = sb("squares", [P, 6])
        norms = sb("norms", [P, 2])
        roots = sb("roots", [P, 2])
        inverse = sb("inverse", [P, 2])
        gain = sb("gain", [P, 2])
        left = sb("left", [P, 16])
        right = sb("right", [P, 8])
        products = sb("products", [P, 2, 4, 4])
        coef = sb("coef", [P, 2, 4])
        gw_rms = sb("gw_rms", [P, 4, EXPERTS])
        gw_prod = sb("gw_prod", [P, 2, EXPERTS, 4])
        mix = sb("mix", [P, KH, XW])

        x1 = sb("x1", [P, TILES, XW])
        sq_junk = sb("sq_junk", [P, 2, H])
        ssum = sb("ssum", [P, TILES])
        rms = sb("rms", [P, TILES])
        rstd = sb("rstd", [P, TILES])
        logit = sb("logit", [P, TILES, EXPERTS])
        shifted = sb("shifted", [P, TILES, EXPERTS])
        top_logit = sb("top_logit", [P, TILES])
        expo = sb("expo", [P, TILES, EXPERTS])
        esum = sb("esum", [P, TILES])
        einv = sb("einv", [P, TILES])
        gatew = sb("gatew", [P, TILES, EXPERTS])
        topw = sb("topw", [P, TILES, 8])
        topi = sb("topi", [P, TILES, 8], u32)
        chosen = sb("chosen", [P, TOP, TILES, EXPERTS])
        mask = sb("mask", [P, TILES, EXPERTS], bf16)
        before_bf = sb("before_bf", [P, P], bf16)
        ones_bf = sb("ones_bf", [P, P], bf16)
        cnt_up = sb("cnt_up", [P, EXPERTS], i32)
        cnt_sh = sb("cnt_sh", [P, EXPERTS], i32)
        ncol_i = sb("ncol_i", [P, EXPERTS], i32)
        wide_i = sb("wide_i", [P, EXPERTS], i32)
        odd_i = sb("odd_i", [P, EXPERTS], i32)
        ntile = sb("ntile", [P, EXPERTS])
        upto = sb("upto", [P, EXPERTS])
        base = sb("base", [P, EXPERTS])
        wide_end = sb("wide_end", [P, EXPERTS])
        entries = sb("entries", [P, EXPERTS])
        table = sb("table", [P, EXPERTS + 1], i32)
        total = sb("total", [P, 1], i32)
        pos = sb("pos", [P, TILES, EXPERTS])
        posm = sb("posm", [P, TOP, TILES, EXPERTS])
        slot_f = sb("slot_f", [P, PICKS])
        slot = sb("slot", [P, PICKS], i32)
        slot_col = sb("slot_col", [P, PICKS], i32)
        slot_row = sb("slot_row", [P, PICKS], i32)
        is_row = xT_sb[:, :, :].rearrange("p k (n c) -> p (k n) c", c=P)
        acts = sb("acts", [P, 2, KM, WIDE])
        is_col = acts[:, :, :, :].rearrange("p l m s -> p (l m s)")[:, 0:PICKS * COLS]\
            .rearrange("p (n c) -> p n c", c=COLS)
        carried = sb("carried", [P, PICKS, 2 * COLS])
        slot_w = sb("slot_w", [P, COLS])
        slot_tok = sb("slot_tok", [P, COLS])
        pad_row = sb("pad_row", [P, COLS])
        slot_idx = sb("slot_idx", [P, COLS], i32)
        zeros = sb("zeros", [P, H])

        gather_idx = sb("gather_idx", [P, 2], i32)
        scatter_idx = sb("scatter_idx", [P, 2], i32)
        xg = sb("xg", [P, 2, H])
        xs_hi = sb("xs_hi", [P, KH, WIDE], f32r)
        xs_lo = sb("xs_lo", [P, KH, WIDE], f32r)
        h1, h2 = acts[:, 0], acts[:, 1]
        h1_hi, h1_lo = sb("h1_hi", [P, KM, WIDE], f32r), sb("h1_lo", [P, KM, WIDE], f32r)
        h2_hi, h2_lo = sb("h2_hi", [P, KM, WIDE], f32r), sb("h2_lo", [P, KM, WIDE], f32r)
        bias_cur = sb("bias_cur", [P, 2 * KM])
        b3w = sb("b3w", [P, 2, H])
        yw = sb("yw", [P, 2, H])

        def bank(name):
            return ctx.enter_context(nc.psum_tensor(name, [P, 512], f32))

        ps_x = bank("ps_x")
        ps_h1 = [bank("ps_h1a"), bank("ps_h1b")]
        ps_h2 = [bank(f"ps_h2{m}") for m in range(KM)]
        ps_y = bank("ps_y")
        ps_x1 = ps_h1
        ps_rank, ps_ctx, ps_slots = ps_h2[0], ps_h2[1], ps_h2[2]

        def small_c(name):
            return small_sb[:, S[name][0]:S[name][1]]

        def cst(name):
            return cst_sb[:, C[name][0]:C[name][1]]

        small_in = sem("small_in")
        cst_in = sem("cst_in")
        ctx_in_sem = sem("ctx_loaded")
        XCH = 4
        x_in = [sem(f"x_in{n}") for n in range(XCH)]
        w_in = [sem("w_in_even"), sem("w_in_odd")]
        bias_in = sem("bias_in")
        b3_in = sem("b3_in")
        first_hi = sem("first_hi")
        whi_ready = sem("whi_ready")
        wlo_ready = sem("wlo_ready")
        rows_out = sem("rows_out")
        resid_out = sem("resid_out")
        dve_step = sem("dve_step")
        act_step = sem("act_step")
        norms_ready = sem("norms_ready")
        mix_ready = sem("mix_ready")
        bf_ready = sem("bf_ready")
        ctx_ready = sem("ctx_ready")
        x1_done = sem("x1_done")
        x1_copied = sem("x1_copied")
        ss_ready = sem("ss_ready")
        rms_ready = sem("rms_ready")
        shifted_ready = sem("shifted_ready")
        exp_ready = sem("exp_ready")
        mask_ready = sem("mask_ready")
        rank_done = sem("rank_done")
        table_ready = sem("table_ready")
        onehot_ready = sem("onehot_ready")
        slots_done = sem("slots_done")
        idx_ready = sem("idx_ready")
        zero_ready = sem("zero_ready")
        gidx_ready = sem("gidx_ready")
        gathered = sem("gathered")
        xpose_done = sem("xpose_done")
        xs_hi_ready = sem("xs_hi_ready")
        xs_ready = sem("xs_ready")
        h1_act = sem("h1_act")
        h2_act = sem("h2_act")
        h1_hi_ready = sem("h1_hi_ready")
        h2_hi_ready = sem("h2_hi_ready")
        l1_done = sem("l1_done")
        h1_ready = sem("h1_ready")
        l2_done = sem("l2_done")
        h2_ready = sem("h2_ready")
        l3_done = sem("l3_done")
        bias_ready = sem("bias_ready")
        b3w_ready = sem("b3w_ready")
        y_ready = sem("y_ready")
        sidx_ready = sem("sidx_ready")
        pool_fence = sem("pool_fence")
        scattered = sem("scattered")

        block = ctx.enter_context(nc.Block())

        def expert_tiles(eng, body, head=None):
            eng.wait_ge(table_ready, 1)
            entry = eng.alloc_register(f"entry_{eng.engine.name}")
            eng.reg_load(entry, table[0:1, 0:1])
            with eng.Fori(0, EXPERTS // 2) as pair:
                for par in range(2):
                    e = pair * 2 + par
                    if head is not None:
                        head(pair, par)
                    word = eng.snap(entry)
                    first = nc.s_assert_within(word & 255, 0, MAX_TILES - 1)
                    wide_end = nc.s_assert_within((word >> WIDE_END_BIT) & 255, 0, MAX_TILES)

                    def ahead():
                        eng.reg_load(entry, table[0:1, bass.ds(e + 1, 1)])

                    with eng.If(first < wide_end):
                        with eng.Fori(first, wide_end) as g:
                            body(Tile(g, pair, e, first), par, WIDE, ahead)
                    with eng.If((word >> NARROW_BIT) > 0):
                        body(Tile(wide_end, pair, e, first), par, P, ahead)

        @block.sync
        def _(sp):
            sp.dma_start(small_sb[:, :], small).then_inc(small_in, 16)
            sp.dma_start(cst_sb[:, :], cst_in_ap).then_inc(cst_in, 16)
            sp.dma_start(ctx_sb[:, :], ctx_in).then_inc(ctx_in_sem, 16)
            n = TOKENS // XCH
            for c in range(XCH):
                sp.dma_start(xT_sb[:, :, c * n:(c + 1) * n],
                             xT[:, c * n:(c + 1) * n].rearrange("(k p) t -> p k t", p=P)).then_inc(x_in[c], 16)
            sp.dma_start(w_raw[:, 0, :], wpack[0, :, :]).then_inc(w_in[0], 16)
            sp.dma_start(w_raw[:, 1, :], wpack[1, :, :]).then_inc(w_in[1], 16)
            sp.dma_start(bias_sb[:, :, :], bpack).then_inc(bias_in, 16)
            sp.dma_start(b3_sb[:, :, :], b3.rearrange("(o e) h -> o e h", o=1).to_broadcast([P, EXPERTS, H]))\
                .then_inc(b3_in, 16)
            sp.wait_ge(zero_ready, 1)
            for dst, done in ((x1_rows, rows_out), (out, resid_out)):
                sp.dma_start(dst[TOKENS:ROWS, :].rearrange("(s p) h -> p s h", p=P),
                             zeros[:, :].rearrange("p (a h) -> p a h", a=1).to_broadcast([P, PAD_SETS, H]))\
                    .then_inc(done, 16)
            q = TILES // XCH
            for c in range(XCH):
                sp.wait_ge(x1_copied, (c + 1) * q)
                for dst, done in ((x1_rows, rows_out), (out, resid_out)):
                    sp.dma_start(dst[c * q * P:(c + 1) * q * P, :].rearrange("(t p) h -> p t h", p=P),
                                 x1[:, c * q:(c + 1) * q, 0:H]).then_inc(done, 16)
            with sp.Fori(1, EXPERTS // 2) as pair:
                for par in range(2):
                    e = pair * 2 + par
                    sp.wait_ge(wlo_ready, e * 2 - 2)
                    sp.dma_start(w_raw[:, par, :], wpack[bass.ds(e, 1), :, :].rearrange("o p w -> (o p) w"))\
                        .then_inc(w_in[par], 16)

        @block.gpsimd
        def _(pool):
            pool.memset(zeros[:, :], 0.0).then_inc(zero_ready, 1)
            pool.wait_ge(idx_ready, 1)

            def gather(g):
                nc.gpsimd.tensor_copy(gather_idx[:, :], slot_idx[:, bass.ds(g * 2, 2)]).then_inc(gidx_ready, 1)
                pool.wait_ge(rows_out, 16 * (XCH + 1))
                pool.wait_ge(gidx_ready, g + 1)
                pool.sem_inc(pool_fence, 1)
                for k in range(2):
                    nc.gpsimd.indirect_dma_start(
                        out=xg[:, k, :], out_offset=None, in_=x1_rows,
                        in_offset=bass.IndirectOffsetOnAxis(ap=gather_idx[:, k:k + 1].bitcast(u32), axis=0))\
                        .then_inc(gathered, 16)

            gather(0)
            pool.wait_ge(resid_out, 16 * (XCH + 1))
            for k in range(2):
                nc.gpsimd.indirect_dma_start(
                    out=out, out_offset=bass.IndirectOffsetOnAxis(
                        ap=slot_idx[:, COLS - 2 + k:COLS - 1 + k].bitcast(u32), axis=0),
                    in_=zeros[:, :], in_offset=None, compute_op=ALU.add).then_inc(scattered, 16)
            pool.wait_ge(xpose_done, 1)
            pool.wait_ge(gathered, 32)
            gather(1)
            pool.wait_ge(b3_in, 16)

            def body(tile, par, width, ahead):
                g = tile.g
                nc.gpsimd.tensor_tensor(b3w[:, :, :], b3_sb[:, bass.ds(tile.expert, 1), :].to_broadcast([P, 2, H]),
                                        slot_w[:, bass.ds(g * 2, 2)].rearrange("p (k a) -> p k a", a=1)
                                        .to_broadcast([P, 2, H]), ALU.mult).then_inc(b3w_ready, 1)
                pool.wait_ge(xpose_done, g + 2)
                pool.wait_ge(gathered, g * 32 + 64)
                gather(g + 2)
                pool.wait_ge(scattered, g * 32 + 32)
                nc.gpsimd.tensor_copy(scatter_idx[:, :], slot_idx[:, bass.ds(g * 2, 2)]).then_inc(sidx_ready, 1)
                with pool.If(tile.g == tile.first):
                    ahead()
                pool.wait_ge(sidx_ready, g + 1)
                pool.wait_ge(resid_out, 16 * (XCH + 1))
                pool.wait_ge(y_ready, g + 2)
                pool.sem_inc(pool_fence, 1)
                for k in range(2):
                    nc.gpsimd.indirect_dma_start(
                        out=out, out_offset=bass.IndirectOffsetOnAxis(ap=scatter_idx[:, k:k + 1].bitcast(u32), axis=0),
                        in_=yw[:, k, :], in_offset=None, compute_op=ALU.add).then_inc(scattered, 16)

            expert_tiles(pool, body)
            tiles = pool.value_load(total[0:1, 0:1], min_val=1, max_val=MAX_TILES)
            pool.wait_ge(scattered, tiles * 32 + 32)
            pool.wait_ge(gathered, tiles * 32 + 64)

        @block.scalar
        def _(act):
            act.wait_ge(cst_in, 16)
            act.wait_ge(norms_ready, 1)
            nc.scalar.activation(roots[:, :], norms[:, :], ACT.Sqrt, bias=cst("eps")[:, 0:1]).then_inc(act_step, 1)
            for t in range(TILES):
                act.wait_ge(x1_copied, t + 1)
                if t >= 2:
                    act.wait_ge(ss_ready, t - 1)
                nc.scalar.activation(sq_junk[:, t % 2, :], x1[:, t, 0:H], ACT.Square,
                                     accum_out=ssum[:, t:t + 1]).then_inc(ss_ready, 1)
                if t >= TILES - FIRST_STEPS:
                    act.wait_ge(w_in[0], 16)
                    n, w = t - (TILES - FIRST_STEPS), PACK // FIRST_STEPS
                    nc.scalar.activation(w_hi[:, 0, n * w:(n + 1) * w], w_raw[:, 0, n * w:(n + 1) * w], ACT.Copy)\
                        .then_inc(first_hi, 1)
            act.wait_ge(ss_ready, TILES)
            nc.scalar.activation(rms[:, :], ssum[:, :], ACT.Sqrt, bias=cst("eps")[:, 1:2],
                                 scale=1.0 / H).then_inc(rms_ready, 1)
            act.wait_ge(shifted_ready, 1)
            nc.scalar.activation(expo[:, :, :], shifted[:, :, :], ACT.Exp).then_inc(exp_ready, 1)
            def weight_highs(tile, par, step, ahead=None):
                with act.If(tile.g == tile.first):
                    if ahead is not None:
                        ahead()
                    with act.If(tile.expert < EXPERTS - 1):
                        at = slice(*STEPS[step])
                        act.wait_ge(w_in[1 - par], tile.pair * 16 + 16 * (1 + par))
                        nc.scalar.activation(w_hi[:, 1 - par, at], w_raw[:, 1 - par, at], ACT.Copy)\
                            .then_inc(whi_ready, 1)

            act.wait_ge(bias_in, 16)

            def body(tile, par, width, ahead):
                g = tile.g
                for m in range(KM):
                    act.wait_ge(l1_done, g * KM + (m + 1))
                    nc.scalar.activation(h1[:, m, 0:width], ps_h1[m % 2][:, 0:width], ACT.Relu,
                                         bias=bias_cur[:, m:m + 1]).then_inc(h1_act, 1)
                weight_highs(tile, par, 0, ahead)
                for m in range(KM):
                    act.wait_ge(l2_done, g * KM + (m + 1))
                    nc.scalar.activation(h2[:, m, 0:width], ps_h2[m][:, 0:width], ACT.Relu,
                                         bias=bias_cur[:, KM + m:KM + m + 1]).then_inc(h2_act, 1)
                act.wait_ge(h2_act, g * KM + KM)
                act.wait_ge(xpose_done, g + 2)
                nc.scalar.activation(xs_hi[:, :, :], ps_x[:, :].rearrange("p (k s) -> p k s", k=KH), ACT.Copy)\
                    .then_inc(xs_hi_ready, 1)
                weight_highs(tile, par, 1)

            act.wait_ge(xpose_done, 1)
            nc.scalar.activation(xs_hi[:, :, :], ps_x[:, :].rearrange("p (k s) -> p k s", k=KH), ACT.Copy)\
                .then_inc(xs_hi_ready, 1)

            def head(pair, par):
                nc.scalar.activation(bias_cur[:, :], bias_sb[:, bass.ds(pair * 2 + par, 1), :]
                                     .rearrange("p o b -> p (o b)"), ACT.Copy).then_inc(bias_ready, 1)
                act.wait_ge(bias_ready, pair * 2 + (par + 1))

            expert_tiles(act, body, head)

        @block.vector
        def _(dve):
            steps = [0]

            def link(ins):
                steps[0] += 1
                ins.then_inc(dve_step, 1)
                dve.wait_ge(dve_step, steps[0])

            V = nc.vector
            dve.wait_ge(small_in, 16)
            link(V.tensor_tensor(squares[:, :], small_sb[:, 0:6], small_sb[:, 0:6], ALU.mult))
            V.tensor_reduce(norms[:, 0:1], squares[:, 0:2], AX, ALU.add)
            V.tensor_reduce(norms[:, 1:2], squares[:, 2:6], AX, ALU.add).then_inc(norms_ready, 1)
            dve.wait_ge(cst_in, 16)
            link(V.tensor_tensor(left[:, :], small_c("lx"), cst("lsign"), ALU.mult))
            link(V.tensor_tensor(right[:, :], small_c("q"), cst("rsign"), ALU.mult))
            link(V.tensor_tensor(
                products[:, :, :, :],
                left[:, :].rearrange("p (a i k) -> p a i k", a=1, i=4).to_broadcast([P, 2, 4, 4]),
                right[:, :].rearrange("p (b a k) -> p b a k", b=2, a=1).to_broadcast([P, 2, 4, 4]), ALU.mult))
            link(V.tensor_reduce(coef[:, :, :], products[:, :, :, :], AX, ALU.add))
            dve.wait_ge(act_step, 1)
            link(V.reciprocal(inverse[:, :], roots[:, :]))
            link(V.tensor_tensor(gain[:, 0:1], inverse[:, 0:1], inverse[:, 1:2], ALU.mult))
            link(V.tensor_tensor(gain[:, 1:2], gain[:, 0:1], small_c("gain"), ALU.mult))
            link(V.scalar_tensor_tensor(coef[:, :, :], coef[:, :, :], gain[:, 1:2],
                                        cst("same").rearrange("p (b i) -> p b i", b=2), ALU.mult, ALU.add))
            link(V.tensor_tensor(
                mix[:, :, 0:H].rearrange("p b (i d) -> p b i d", i=4),
                cst("diag").rearrange("p (a c d) -> p a c d", a=1, c=1).to_broadcast([P, 2, 4, QD]),
                coef[:, :, :].rearrange("p b (i a) -> p b i a", a=1).to_broadcast([P, 2, 4, QD]), ALU.mult))
            link(V.tensor_tensor(gw_rms[:, :, :], small_c("wg").rearrange("p (i e) -> p i e", i=4),
                                 small_c("rms").rearrange("p (i a) -> p i a", a=1).to_broadcast([P, 4, EXPERTS]),
                                 ALU.mult))
            link(V.tensor_tensor(
                gw_prod[:, :, :, :],
                gw_rms[:, :, :].rearrange("p i (a e) -> p a e i", a=1).to_broadcast([P, 2, EXPERTS, 4]),
                coef[:, :, :].rearrange("p b (a i) -> p b a i", a=1).to_broadcast([P, 2, EXPERTS, 4]), ALU.mult))
            V.tensor_reduce(mix[:, :, H:XW], gw_prod[:, :, :, :], AX, ALU.add).then_inc(mix_ready, 1)
            V.tensor_copy(before_bf[:, :], cst("before")).then_inc(bf_ready, 1)
            V.tensor_copy(ones_bf[:, :], cst("ones")).then_inc(bf_ready, 1)

            def first_lows(n):
                dve.wait_ge(first_hi, n + 1)
                w = PACK // FIRST_STEPS
                ins = V.tensor_tensor(w_lo[:, 0, n * w:(n + 1) * w], w_raw[:, 0, n * w:(n + 1) * w],
                                      w_hi[:, 0, n * w:(n + 1) * w].bitcast(f32), ALU.subtract)
                if n % (FIRST_STEPS // 2) == FIRST_STEPS // 2 - 1:
                    ins.then_inc(wlo_ready, 1)

            for t in range(TILES):
                dve.wait_ge(x1_done, t + 1)
                V.tensor_copy(x1[:, t, :], ps_x1[t % 2][:, 0:XW]).then_inc(x1_copied, 1)
                if t >= TILES - FIRST_STEPS + 1:
                    first_lows(t - (TILES - FIRST_STEPS + 1))
            first_lows(FIRST_STEPS - 1)

            dve.wait_ge(x1_copied, TILES)
            dve.wait_ge(rms_ready, 1)
            link(V.reciprocal(rstd[:, :], rms[:, :]))

            def over_experts(ap):
                return ap.rearrange("p (t a) -> p t a", a=1).to_broadcast([P, TILES, EXPERTS])

            link(V.tensor_tensor(logit[:, :, :], x1[:, :, H:XW], over_experts(rstd[:, :]), ALU.mult))
            dve.wait_ge(ctx_ready, 1)
            lg = logit[:, :, :].rearrange("p (b t) e -> p b t e", b=BATCH)
            link(V.tensor_tensor(
                lg, lg, ps_ctx[:, 0:BATCH * EXPERTS].rearrange("p (b a e) -> p b a e", b=BATCH, a=1)
                .to_broadcast([P, BATCH, TILES // BATCH, EXPERTS]), ALU.add))
            link(V.tensor_reduce(top_logit[:, :], logit[:, :, :], AX, ALU.max))
            V.tensor_tensor(shifted[:, :, :], logit[:, :, :], over_experts(top_logit[:, :]), ALU.subtract)\
                .then_inc(shifted_ready, 1)
            dve.wait_ge(exp_ready, 1)
            link(V.tensor_reduce(esum[:, :], expo[:, :, :], AX, ALU.add))
            link(V.reciprocal(einv[:, :], esum[:, :]))
            link(V.tensor_tensor(gatew[:, :, :], expo[:, :, :], over_experts(einv[:, :]), ALU.mult))
            for t in range(TILES):
                last = V.max(topw[:, t, :], gatew[:, t, :])
            link(last)
            for t in range(TILES):
                last = V.max_index(topi[:, t, :], topw[:, t, :], gatew[:, t, :])
            link(last)
            iota = cst("iota")
            link(V.tensor_tensor(
                chosen[:, :, :, :],
                iota[:, 0:EXPERTS].rearrange("p (a b e) -> p a b e", a=1, b=1).to_broadcast([P, TOP, TILES, EXPERTS]),
                topi[:, :, 0:TOP].rearrange("p t (k a) -> p k t a", a=1).to_broadcast([P, TOP, TILES, EXPERTS]),
                ALU.is_equal))
            V.tensor_tensor(mask[:, :, :], chosen[:, 0, :, :], chosen[:, 1, :, :], ALU.add).then_inc(mask_ready, 1)
            dve.wait_ge(rank_done, 1)
            link(V.tensor_scalar(cnt_up[:, :], ps_rank[:, TILES * EXPERTS:(TILES + 1) * EXPERTS],
                                 float(P - 1), None, ALU.add))
            link(V.tensor_scalar(cnt_sh[:, :], cnt_up[:, :], 7, None, ALU.logical_shift_right))
            link(V.tensor_scalar(ncol_i[:, :], cnt_sh[:, :], 1.0, None, ALU.max))
            V.tensor_scalar(wide_i[:, :], ncol_i[:, :], 1, None, ALU.logical_shift_right)
            link(V.tensor_scalar(odd_i[:, :], ncol_i[:, :], 1, None, ALU.bitwise_and))
            link(V.tensor_tensor(ntile[:, :], wide_i[:, :], odd_i[:, :], ALU.add))
            link(V.tensor_tensor_scan(upto[:, :], cst("ones")[:, 0:EXPERTS], ntile[:, :], 0.0, ALU.mult, ALU.add))
            V.tensor_tensor(base[:, :], upto[:, :], ntile[:, :], ALU.subtract)
            V.tensor_copy(total[:, :], upto[:, EXPERTS - 1:EXPERTS])
            link(V.tensor_tensor(wide_end[:, :], upto[:, :], odd_i[:, :], ALU.subtract))
            link(V.scalar_tensor_tensor(entries[:, :], wide_end[:, :], float(1 << WIDE_END_BIT), base[:, :],
                                        ALU.mult, ALU.add))
            V.memset(table[:, EXPERTS:EXPERTS + 1], 0)
            V.scalar_tensor_tensor(table[:, 0:EXPERTS], odd_i[:, :], float(1 << NARROW_BIT), entries[:, :],
                                   ALU.mult, ALU.add).then_inc(table_ready, 1)
            link(V.scalar_tensor_tensor(
                pos[:, :, :], base[:, :].rearrange("p (a e) -> p a e", a=1).to_broadcast([P, TILES, EXPERTS]),
                float(WIDE), ps_rank[:, 0:TILES * EXPERTS].rearrange("p (t e) -> p t e", e=EXPERTS),
                ALU.mult, ALU.add))
            link(V.tensor_tensor(
                posm[:, :, :, :], chosen[:, :, :, :],
                pos[:, :, :].rearrange("p (a t) e -> p a t e", a=1).to_broadcast([P, TOP, TILES, EXPERTS]), ALU.mult))
            link(V.tensor_reduce(slot_f[:, :].rearrange("p (k t) -> p k t", k=TOP), posm[:, :, :, :], AX, ALU.add))
            link(V.tensor_copy(slot[:, :], slot_f[:, :]))
            link(V.tensor_scalar(slot_col[:, :], slot[:, :], 7, None, ALU.logical_shift_right))
            link(V.tensor_scalar(slot_row[:, :], slot[:, :], P - 1, None, ALU.bitwise_and))
            link(V.tensor_tensor(
                is_col[:, :, :], iota[:, 0:COLS].rearrange("p (a c) -> p a c", a=1).to_broadcast([P, PICKS, COLS]),
                slot_col[:, :].rearrange("p (n a) -> p n a", a=1).to_broadcast([P, PICKS, COLS]), ALU.is_equal))
            for k in range(TOP):
                n0, n1 = k * TILES, (k + 1) * TILES
                V.tensor_tensor(carried[:, n0:n1, 0:COLS], is_col[:, n0:n1, :],
                                cst("token").rearrange("p (t a) -> p t a", a=1).to_broadcast([P, TILES, COLS]),
                                ALU.mult)
                V.tensor_tensor(carried[:, n0:n1, COLS:2 * COLS], is_col[:, n0:n1, :],
                                topw[:, :, k:k + 1].to_broadcast([P, TILES, COLS]), ALU.mult)
            for n in range(PICKS):
                V.tensor_scalar(is_row[:, n, :], iota, slot_row[:, n:n + 1], None, ALU.is_equal)\
                    .then_inc(onehot_ready, 1)
            dve.wait_ge(slots_done, 1)
            link(V.scalar_tensor_tensor(pad_row[:, :], ps_slots[:, 0:COLS], 0.0, cst("pad"), ALU.is_equal, ALU.mult))
            V.tensor_copy(slot_w[:, :], ps_slots[:, COLS:2 * COLS])
            V.scalar_tensor_tensor(slot_idx[:, :], ps_slots[:, 0:COLS], -1.0, pad_row[:, :], ALU.add, ALU.add)\
                .then_inc(idx_ready, 1)

            def x_lows():
                V.tensor_tensor(xs_lo[:, :, :], ps_x[:, :].rearrange("p (k s) -> p k s", k=KH),
                                xs_hi[:, :, :].bitcast(f32), ALU.subtract).then_inc(xs_ready, 1)

            V.memset(yw[:, 1, :], 0.0)
            dve.sem_inc(y_ready, 1)
            dve.wait_ge(xs_hi_ready, 1)
            x_lows()

            def weight_lows(tile, par, step, ahead=None):
                with dve.If(tile.g == tile.first):
                    if ahead is not None:
                        ahead()
                    with dve.If(tile.expert < EXPERTS - 1):
                        at = slice(*STEPS[step])
                        dve.wait_ge(whi_ready, tile.expert * 2 + (step + 1))
                        V.tensor_tensor(w_lo[:, 1 - par, at], w_raw[:, 1 - par, at],
                                        w_hi[:, 1 - par, at].bitcast(f32), ALU.subtract).then_inc(wlo_ready, 1)

            def split(src, hi, lo, done, hi_ready, ready, g, width):
                for m in range(KM):
                    dve.wait_ge(done, g * KM + (m + 1))
                    V.tensor_copy(hi[:, m, 0:width], src[:, m, 0:width]).then_inc(hi_ready, 1)
                    dve.wait_ge(hi_ready, g * KM + (m + 1))
                    V.tensor_tensor(lo[:, m, 0:width], src[:, m, 0:width], hi[:, m, 0:width].bitcast(f32),
                                    ALU.subtract).then_inc(ready, 1)

            def body(tile, par, width, ahead):
                g = tile.g
                split(h1, h1_hi, h1_lo, h1_act, h1_hi_ready, h1_ready, g, width)
                weight_lows(tile, par, 0, ahead)
                split(h2, h2_hi, h2_lo, h2_act, h2_hi_ready, h2_ready, g, width)
                dve.wait_ge(xs_hi_ready, g + 2)
                x_lows()
                weight_lows(tile, par, 1)
                dve.wait_ge(b3w_ready, g + 1)
                dve.wait_ge(l3_done, g + 1)
                dve.wait_ge(scattered, g * 32 + 32)
                for k in range(width // P):
                    last = V.scalar_tensor_tensor(yw[:, k, :], ps_y[:, k * H:(k + 1) * H],
                                                  slot_w[:, bass.ds(g * 2 + k, 1)], b3w[:, k, :], ALU.mult, ALU.add)
                last.then_inc(y_ready, 1)

            expert_tiles(dve, body)

        @block.tensor
        def _(pe):
            ident = cst("ident")
            pe.wait_ge(cst_in, 16)
            pe.wait_ge(ctx_in_sem, 16)
            for b in range(BATCH):
                last = nc.tensor.matmul(ps_ctx[:, b * EXPERTS:(b + 1) * EXPERTS], ctx_sb[:, b * P:(b + 1) * P],
                                        ctx_sb[:, BATCH * P:BATCH * P + EXPERTS], start=True, stop=True)
            last.then_inc(ctx_ready, 1)
            pe.wait_ge(mix_ready, 1)
            for t in range(TILES):
                if t % (TILES // XCH) == 0:
                    pe.wait_ge(x_in[t // (TILES // XCH)], 16)
                if t >= 2:
                    pe.wait_ge(x1_copied, t - 1)
                for k in range(KH):
                    last = nc.tensor.matmul(ps_x1[t % 2][:, 0:XW], xT_sb[:, k, t * P:(t + 1) * P], mix[:, k, :],
                                            start=(k == 0), stop=(k == KH - 1))
                last.then_inc(x1_done, 1)
            pe.wait_ge(mask_ready, 1)
            pe.wait_ge(bf_ready, 2)
            nc.tensor.matmul(ps_rank[:, 0:TILES * EXPERTS], before_bf[:, :], mask[:, :, :], start=True, stop=False,
                             skip_group_check=True)
            for t in range(TILES):
                last = nc.tensor.matmul(
                    ps_rank[:, (t + 1) * EXPERTS:(TILES + 1) * EXPERTS].rearrange("p (t e) -> p t e", e=EXPERTS),
                    ones_bf[:, :], mask[:, t:t + 1, :].to_broadcast([P, TILES - t, EXPERTS]),
                    start=False, stop=(t == TILES - 1), skip_group_check=True)
            last.then_inc(rank_done, 1)
            for n in range(PICKS):
                pe.wait_ge(onehot_ready, n + 1)
                last = nc.tensor.matmul(ps_slots[:, 0:2 * COLS], is_row[:, n, :], carried[:, n, :],
                                        start=(n == 0), stop=(n == PICKS - 1))
            last.then_inc(slots_done, 1)

            def transpose_x():
                for kb in range(KH):
                    for k in range(2):
                        last = nc.tensor.transpose(ps_x[:, kb * WIDE + k * P:kb * WIDE + (k + 1) * P],
                                                   xg[:, k, kb * P:(kb + 1) * P], ident)
                last.then_inc(xpose_done, 1)

            pe.wait_ge(gathered, 32)
            transpose_x()

            def product(dst, w_at, par, act_hi, act_lo, start, stop, weights_move=False, **more):
                wh, wl = w_hi[:, par, w_at], w_lo[:, par, w_at]
                terms = [(wh, act_hi), (wh, act_lo), (wl, act_hi)]
                for n, (w, a) in enumerate(terms):
                    still, move = (a, w) if weights_move else (w, a)
                    last = nc.tensor.matmul(dst, still, move, start=(start and n == 0),
                                            stop=(stop and n == len(terms) - 1), **more)
                return last

            def body(tile, par, width, ahead):
                g = tile.g
                pe.wait_ge(wlo_ready, tile.expert * 2 + 2)
                pe.wait_ge(xs_ready, g + 1)
                for m in range(KM):
                    if m >= 2:
                        pe.wait_ge(h1_act, g * KM + (m - 1))
                    for k in range(KH):
                        o = O_W1 + k * M + m * P
                        last = product(ps_h1[m % 2][:, 0:width], slice(o, o + P), par, xs_hi[:, k, 0:width],
                                       xs_lo[:, k, 0:width], k == 0, k == KH - 1)
                    last.then_inc(l1_done, 1)
                half = KM // 2
                for ks, ms in [((k,), range(KM)) for k in range(half)] + [(range(half, KM), (m,)) for m in range(KM)]:
                    for m in ms:
                        for k in ks:
                            if m == 0:
                                pe.wait_ge(h1_ready, g * KM + (k + 1))
                            o = O_W2 + k * M + m * P
                            last = product(ps_h2[m][:, 0:width], slice(o, o + P), par, h1_hi[:, k, 0:width],
                                           h1_lo[:, k, 0:width], k == 0, k == KM - 1)
                        if ks[-1] == KM - 1:
                            last.then_inc(l2_done, 1)
                with pe.If(tile.g == tile.first):
                    ahead()
                pe.wait_ge(gathered, g * 32 + 64)
                transpose_x()
                pe.wait_ge(y_ready, g + 1)
                for k in range(KM):
                    pe.wait_ge(h2_ready, g * KM + (k + 1))
                    for s in range(width // P):
                        o = O_W3 + k * H
                        last = product(ps_y[:, s * H:(s + 1) * H], slice(o, o + H), par,
                                       h2_hi[:, k, s * P:(s + 1) * P], h2_lo[:, k, s * P:(s + 1) * P],
                                       k == 0 and s == 0, k == KM - 1, weights_move=True, skip_group_check=True)
                last.then_inc(l3_done, 1)

            expert_tiles(pe, body)



def constants():
    import numpy as np
    S, n = columns(CONST)
    c = np.zeros((P, n), np.float32)

    def put(name, v):
        c[:, S[name][0]:S[name][1]] = v

    p = np.arange(P)
    put("ident", np.eye(P))
    put("before", p[:, None] < p[None, :])
    put("ones", 1.0)
    put("diag", (p[:, None] % QD) == np.arange(QD)[None, :])
    put("iota", p[None, :])
    put("token", np.arange(TILES)[None, :] * P + p[:, None] + 1)
    put("pad", TOKENS + 1 + p[:, None] + P * (np.arange(COLS)[None, :] % 2))
    ls = np.array([[1, -1, -1, -1], [1, 1, -1, 1], [1, 1, 1, -1], [1, -1, 1, 1]])
    rs = np.array([[1, -1, -1, -1], [1, 1, 1, -1], [1, -1, 1, 1], [1, 1, -1, 1]])
    conj = np.array([1, -1, -1, -1])
    put("lsign", ls.reshape(1, 16))
    j = 2 * np.arange(2)[None, :, None] + (p // QD)[:, None, None]
    k = np.arange(4)[None, None, :]
    put("rsign", (rs[k, j] * conj[k ^ j]).reshape(P, 8))
    put("same", (k == j).reshape(P, 8))
    put("eps", np.array([1e-8, 1e-6]))
    return c


def kernel(**inputs):
    import numpy as np
    import concourse.bacc as bacc
    from concourse.bass_utils import run_bass_kernel_spmd

    a = {k: np.asarray(v) for k, v in inputs.items()}
    x, cond = a["x"], a["cond_256"]
    d = np.arange(P) % QD
    half = np.arange(P) // QD
    row = np.minimum(np.arange(4), BATCH - 1)
    i, k = np.arange(4)[:, None], np.arange(4)[None, :]
    j = 2 * np.arange(2)[None, :, None] + half[:, None, None]
    q = a["L0_cond_q_right"][np.arange(4)[None, None, :] ^ j, d[:, None, None]].reshape(P, 8)
    lx = cond[row[i ^ k][None], d[:, None, None]].reshape(P, 16)
    rms = a["L1_cond_rms_w"].reshape(4, QD)[:, d].T
    wg = a["L1_cond_wg_W"].reshape(4, QD, EXPERTS)[:, d].transpose(1, 0, 2).reshape(P, 4 * EXPERTS)
    small = np.concatenate([cond[:, d].T, q, lx, a["L0_cond_spectral_gate"].reshape(QD)[d][:, None], rms, wg], 1)
    ctx = np.ones((GENRE + 2, BATCH * P + EXPERTS), np.float32)
    for b in range(BATCH):
        ctx[:GENRE, b * P:(b + 1) * P] = cond[b][:, None]
    ctx[:GENRE, BATCH * P:] = a["L1_cond_gg_W"]
    ctx[GENRE, BATCH * P:] = a["L1_cond_wg_b"]
    ctx[GENRE + 1, BATCH * P:] = a["L1_cond_gg_b"]

    def blocks(w):
        e, kk, n = w.shape
        return w.reshape(e, kk // P, P, n).transpose(0, 2, 1, 3).reshape(e, P, -1)

    def column(b):
        return b.reshape(EXPERTS, KM, P).transpose(0, 2, 1)

    wpack = np.concatenate([blocks(a["L1_cond_W1"]), blocks(a["L1_cond_W2"]), blocks(a["L1_cond_W3"])], 2)
    bpack = np.concatenate([column(a["L1_cond_b1"]), column(a["L1_cond_b2"])], 2).transpose(1, 0, 2)
    arrays = {"xT": x.reshape(TOKENS, H).T, "small": small, "cst": constants(), "ctx": ctx, "wpack": wpack,
              "bpack": bpack,
              "b3": a["L1_cond_b3"]}
    arrays = {f"in_{n}": np.ascontiguousarray(v) for n, v in arrays.items()}

    nc = bacc.Bacc("TRN2", target_bir_lowering=False, num_devices=1)
    args = [nc.dram_tensor(n, v.shape, mybir.dt.from_np(v.dtype), kind="ExternalInput").ap()
            for n, v in arrays.items()]
    out = nc.dram_tensor("out_rows", (ROWS, H), mybir.dt.float32, kind="ExternalOutput").ap()
    build(nc, *args, out)
    r = run_bass_kernel_spmd(nc, [arrays], core_ids=[0])
    return r.results[0]["out_rows"][:TOKENS].reshape(BATCH, SEQ, H)
```
